# Optimizing a Trainium2 kernel written in Bass

```python
import numpy as np
import jax
import jax.numpy as jnp

def _softmax(x, axis=-1):
    return jax.nn.softmax(x, axis=axis)

def _gelu(x):
    return jax.nn.gelu(x, approximate=True)

def _silu(x):
    return jax.nn.silu(x)

def _sigmoid(x):
    return jax.nn.sigmoid(x)

def _layernorm(x, axis=-1, eps=1e-05):
    m = jnp.mean(x, axis=axis, keepdims=True)
    v = jnp.var(x, axis=axis, keepdims=True)
    return (x - m) / jnp.sqrt(v + eps)

def _scatter_add(tgt, idx, src, axis=0):
    return tgt.at[idx].add(src)

def _segment_sum(src, seg, n):
    return jax.ops.segment_sum(src, seg, n)
kernel_name = 'mk_cond_resid_d2_seqx_r2_cf0125'

def setup_inputs(seed: int=0):
    np.random.seed(seed)
    _w = jnp.asarray

    def _rec_inputs():
        import jax
        import jax.numpy as jnp
        _rk = jax.random.key(seed)
        x = -7.109e-05 + 0.9999 * jax.random.normal(jax.random.fold_in(_rk, 1), (128, 128, 1024), jnp.float32)
        _lenS = 128 - jax.random.randint(jax.random.fold_in(_rk, 7), (128,), 0, max(1, 128 // 4) + 1, jnp.int32)
        _lenS2 = 128 - jax.random.randint(jax.random.fold_in(_rk, 8), (128,), 0, max(1, 128 // 4) + 1, jnp.int32)
        itok_B_0_7 = jax.random.randint(jax.random.fold_in(_rk, 11), (128,), 0, 8, jnp.int32)
        itok_B_0_6 = jax.random.randint(jax.random.fold_in(_rk, 12), (128,), 0, 7, jnp.int32)
        return (x, itok_B_0_7, itok_B_0_6)
    x, itok_B_0_7, itok_B_0_6 = _rec_inputs()

    def _L0_cond_setup():
        import jax, jax.numpy as jnp
        import numpy as np
        B, C, D, T, N_SUBJECTS = (128, 128, 128, 1024, 8)
        key = jax.random.key(seed)
        kx, ks, kw = jax.random.split(key, 3)
        x = jax.random.normal(kx, (B, C, T), dtype=jnp.float32)
        subjects = jax.random.randint(ks, (B,), 0, N_SUBJECTS, dtype=jnp.int64)
        weights = jax.random.normal(kw, (N_SUBJECTS, C, D), dtype=jnp.float32) * (1.0 / C ** 0.5)
        return {'x': x, 'subjects': subjects, 'weights': weights}
    _L0_cond_all = _L0_cond_setup()
    _L0_cond_in = {k: v for k, v in _L0_cond_all.items() if k in ('weights',)}
    del _L0_cond_all

    def _L1_cond_setup():
        import jax, jax.numpy as jnp
        import numpy as np
        B, T, D_IN, D_OUT = (16, 1024, 1024, 1024)
        N_ADAPTERS, RANK = (8, 16)
        key = jax.random.key(seed)
        k_x, k_w, k_a, k_b, k_s, k_idx = jax.random.split(key, 6)
        x = jax.random.normal(k_x, (B, T, D_IN), dtype=jnp.float32)
        W = jax.random.normal(k_w, (D_OUT, D_IN), dtype=jnp.float32) * (1.0 / np.sqrt(D_IN))
        A = jax.random.normal(k_a, (N_ADAPTERS, RANK, D_IN), dtype=jnp.float32) * 0.02
        Bm = jax.random.normal(k_b, (N_ADAPTERS, D_OUT, RANK), dtype=jnp.float32) * 0.02
        scalings = jnp.ones((N_ADAPTERS,), dtype=jnp.float32)
        adapter_idx = jax.random.randint(k_idx, (B,), 0, N_ADAPTERS, dtype=jnp.int32)
        return {'x': x, 'W': W, 'A': A, 'Bm': Bm, 'scalings': scalings, 'adapter_idx': adapter_idx}
    _L1_cond_all = _L1_cond_setup()
    _L1_cond_in = {k: v for k, v in _L1_cond_all.items() if k in ('W', 'A', 'Bm', 'scalings')}
    del _L1_cond_all
    return {'x': x, 'itok_B_0_7': itok_B_0_7, 'itok_B_0_6': itok_B_0_6, 'L0_cond_weights': _L0_cond_in['weights'], 'L1_cond_W': _L1_cond_in['W'], 'L1_cond_A': _L1_cond_in['A'], 'L1_cond_Bm': _L1_cond_in['Bm'], 'L1_cond_scalings': _L1_cond_in['scalings']}

def reference(x, itok_B_0_7, itok_B_0_6, L0_cond_weights, L1_cond_W, L1_cond_A, L1_cond_Bm, L1_cond_scalings):
    import jax
    import jax.numpy as jnp

    def _L0_cond_ref(x, subjects, weights):
        import jax, jax.numpy as jnp
        import numpy as np
        B, C, D, T, N_SUBJECTS = (128, 128, 128, 1024, 8)
        w = weights[subjects]
        out = jnp.einsum('bct,bcd->bdt', x, w)
        return out

    def _L1_cond_ref(x, W, A, Bm, scalings, adapter_idx):
        import jax, jax.numpy as jnp
        import numpy as np
        B, T, D_IN, D_OUT = (16, 1024, 1024, 1024)
        N_ADAPTERS, RANK = (8, 16)
        H = jnp.einsum('btd,od->bto', x, W)
        A_b = A[adapter_idx]
        B_b = Bm[adapter_idx]
        s_b = scalings[adapter_idx]
        xa = jnp.einsum('btd,brd->btr', x, A_b)
        delta = jnp.einsum('btr,bor->bto', xa, B_b)
        delta = jax.lax.stop_gradient(delta * s_b[:, None, None])
        return H + delta
    x = x + _L0_cond_ref(x, itok_B_0_7, L0_cond_weights)
    x = x + _L1_cond_ref(x, L1_cond_W, L1_cond_A, L1_cond_Bm, L1_cond_scalings, itok_B_0_6)
    return x

_drawn_inputs = setup_inputs


def setup_inputs(seed=0):
    import zlib

    import numpy as np

    out = dict(_drawn_inputs(seed))
    spreads = {'L1_cond_scalings': (1.0, 0.2)}
    factors = {}
    for name, (base, spread) in spreads.items():
        noise = np.random.default_rng([zlib.crc32(name.encode()), seed]).standard_normal(out[name].shape)
        drawn = base * np.exp(spread * noise) if base else spread * noise
        out[name] = jnp.asarray(drawn.astype(out[name].dtype))
    for name, factor in factors.items():
        out[name] = (out[name] * factor).astype(out[name].dtype)
    return out
```

```python
from contextlib import ExitStack

import concourse.bass as bass
from concourse import mybir

P = 128
BANK = 512
UNROLL = 4

ALU = mybir.AluOpType
F32 = mybir.dt.float32
F32R = mybir.dt.float32r
I32 = mybir.dt.int32


def cond_resid_kernel(nc, x, subjects, adapters, w0, W, A, Bm, scalings, out):
    NB, C, T = x.shape
    NS, _, D = w0.shape
    O = W.shape[0]
    NA, RANK, _ = A.shape
    KT = T // P
    OT = O // P
    HALVES = O // BANK
    KPB = BANK // P
    YB = KT // KPB
    GROUPS = NB // UNROLL
    QUAD = 2 * RANK
    NQ = P // QUAD
    assert C == D == P and NA * RANK == P and QUAD == 32 and GROUPS >= 3

    with ExitStack() as ctx:
        def sb(name, shape, dt=F32, scope=ctx):
            return scope.enter_context(nc.sbuf_tensor(name, shape, dt))

        def psum(name, shape):
            return ctx.enter_context(nc.psum_tensor(name, shape, F32))

        def sem(name):
            return ctx.enter_context(nc.semaphore(name))

        m_hi = sb("m_hi", [P, KT, O], F32R)
        m_lo = sb("m_lo", [P, KT, O], F32R)
        atab = sb("atab", [P, NA, KT, QUAD], F32R)
        wtab = sb("wtab", [P, NS, 2, D], F32R)
        ident = sb("ident", [P, P])
        ids = sb("ids", [1, 2, NB], I32)
        scale = sb("scale", [P, 1])
        x_in = sb("x_in", [P, UNROLL, T])
        x_hi = sb("x_hi", [P, 2, T], F32R)
        x_lo = sb("x_lo", [P, 2, T], F32R)
        y_hi = sb("y_hi", [P, 2, KT, C], F32R)
        y_lo = sb("y_lo", [P, 2, KT, C], F32R)
        w_now = sb("w_now", [P, 2, 2, D], F32R)
        a_now = sb("a_now", [P, 2, KT, NQ, QUAD], F32R)
        stack = sb("stack", [P, C], F32R)

        with ExitStack() as prep:
            w_raw = sb("w_raw", [P, KT, OT, P], F32, prep)
        b_tab = sb("b_tab", [P, NA, O], F32R)
        with ExitStack() as prep:
            bt_hi = sb("bt_hi", [P, O], F32R, prep)
            bt_lo = sb("bt_lo", [P, O], F32R, prep)
            sel_hi = sb("sel_hi", [P, NA, NQ, 2, RANK], F32R, prep)
            sel_lo = sb("sel_lo", [P, NA, NQ, 2, RANK], F32R, prep)
        z_out = sb("z_out", [P, UNROLL, O])
        with ExitStack() as prep:
            a_raw = sb("a_raw", [P, T], F32, prep)
            w0_raw = sb("w0_raw", [P, NS, D], F32, prep)
        b_now = sb("b_now", [P, 2, O], F32R)
        b_raw = sb("b_raw", [P, NA, OT, RANK])
        b_flat = sb("b_flat", [P, OT, NA, RANK])

        z_ps = psum("z_ps", [P, 2, HALVES, BANK])
        y_ps = psum("y_ps", [P, YB, KPB, C])
        r_ps = psum("r_ps", [P, BANK])

        x_landed = [sem(f"x_landed{u}") for u in range(UNROLL)]
        w_landed = [sem(f"w_landed{k}") for k in range(KT)]
        small_landed = {n: sem(f"{n}_landed") for n in ("ids", "w0", "a", "b")}
        z_stored = [sem(f"z_stored{u}") for u in range(UNROLL)]
        ident_ready = sem("ident_ready")
        w0_biased = sem("w0_biased")
        wtab_hi = sem("wtab_hi")
        wtab_ready = sem("wtab_ready")
        at_turned = sem("at_turned")
        atab_hi = sem("atab_hi")
        atab_ready = sem("atab_ready")
        b_flat_ready = sem("b_flat_ready")
        bt_turned = sem("bt_turned")
        bt_scaled = sem("bt_scaled")
        bt_split = sem("bt_split")
        sel_zeroed = sem("sel_zeroed")
        sel_ready = sem("sel_ready")
        w_turned = sem("w_turned")
        m_biased = sem("m_biased")
        m_hi_ready = sem("m_hi_ready")
        m_ready = sem("m_ready")
        b_spread = sem("b_spread")
        btab_ready = [sem(f"btab_ready{h}") for h in range(HALVES)]
        x_hi_ready = sem("x_hi_ready")
        x_lo_ready = sem("x_lo_ready")
        w_staged = sem("w_staged")
        a_staged = sem("a_staged")
        b_staged = sem("b_staged")
        y_done = sem("y_done")
        y_hi_ready = sem("y_hi_ready")
        y_lo_ready = sem("y_lo_ready")
        r_done = sem("r_done")
        r_hi_ready = sem("r_hi_ready")
        stack_ready = sem("stack_ready")
        z_done = sem("z_done")
        z_copied = [sem(f"z_copied{h}") for h in range(HALVES)]

        MBANKS = KT * HALVES
        RING = 2 * HALVES

        def m_bank(n):
            return z_ps[:, (n % RING) // HALVES, n % HALVES, :]

        block = ctx.enter_context(nc.Block())

        @block.sync
        def _(sp):
            sp.dma_start(w0_raw[:, :, :], w0.rearrange("s c d -> c s d")).then_inc(small_landed["w0"], 16)
            sp.dma_start(x_in[:, 0, :], x[0]).then_inc(x_landed[0], 16)
            sp.dma_start(a_raw[:, :], A.rearrange("a r t -> (a r) t")).then_inc(small_landed["a"], 16)
            for k in range(KT):
                sp.dma_start(w_raw[:, k, :, :],
                             W[:, k * P:(k + 1) * P].rearrange("(n o) t -> o n t", o=P)).then_inc(w_landed[k], 16)
            for b in range(1, UNROLL):
                sp.dma_start(x_in[:, b, :], x[b]).then_inc(x_landed[b], 16)

            def step(g, u, last):
                if not last:
                    sp.wait_ge(x_hi_ready, UNROLL * g + u + 1)
                    sp.wait_ge(x_lo_ready, UNROLL * g + u + 1)
                    sp.dma_start(x_in[:, u, :], x[bass.ds(UNROLL * g + (UNROLL + u), 1), :, :].rearrange("b c t -> (b c) t"))\
                      .then_inc(x_landed[u], 16)
                for h in range(HALVES):
                    sp.wait_ge(z_copied[h], UNROLL * g + u + 1)
                sp.dma_start(out[bass.ds(UNROLL * g + u, 1), :, :].rearrange("b c t -> (b c) t"), z_out[:, u, :])\
                  .then_inc(z_stored[u], 16)

            with sp.Fori(0, GROUPS - 1) as g:
                for u in range(UNROLL):
                    step(g, u, False)
            for u in range(UNROLL):
                step(GROUPS - 1, u, True)
            for u in range(UNROLL):
                sp.wait_ge(z_stored[u], 16 * GROUPS)

        @block.gpsimd
        def _(pool):
            pool.dma_start(ids[0:1, 0, :], subjects.rearrange("(a b) -> a b", a=1)).then_inc(small_landed["ids"], 16)
            pool.dma_start(ids[0:1, 1, :], adapters.rearrange("(a b) -> a b", a=1)).then_inc(small_landed["ids"], 16)
            nc.gpsimd.memset(ident[:, :], 0.0).then_inc(ident_ready, 1)
            pool.wait_ge(ident_ready, 1)
            nc.gpsimd.affine_select(out=ident[:, :], in_=ident[:, :], compare_op=ALU.not_equal, fill=1.0,
                                    base=0, pattern=[[-1, P]], channel_multiplier=1).then_inc(ident_ready, 1)
            nc.gpsimd.memset(sel_hi[:, :, :, :, :].bitcast(F32), 0.0).then_inc(sel_zeroed, 1)
            nc.gpsimd.memset(sel_lo[:, :, :, :, :].bitcast(F32), 0.0).then_inc(sel_zeroed, 1)
            pool.wait_ge(ident_ready, 2)
            pool.wait_ge(sel_zeroed, 2)
            for q in range(NQ):
                sel = sel_hi if q % 2 == 0 else sel_lo
                for half in range(2):
                    nc.gpsimd.tensor_copy(sel[:, :, q, half, :],
                                          ident[:, :].rearrange("p (a r) -> p a r", r=RANK)).then_inc(sel_ready, 1)
            pool.wait_ge(small_landed["b"], 16 * (NA + 1))
            nc.gpsimd.tensor_copy(b_flat[:, :, :, :], b_raw[:, :, :, :].rearrange("p a n r -> p n a r"))\
              .then_inc(b_flat_ready, 1)
            pool.wait_ge(small_landed["ids"], 32)

            def stage(g, u, first):
                slot = u % 2
                again = not (first and u < 2)
                s = pool.value_load(ids[0:1, 0, bass.ds(UNROLL * g + u, 1)], min_val=0, max_val=NS - 1)
                a = pool.value_load(ids[0:1, 1, bass.ds(UNROLL * g + u, 1)], min_val=0, max_val=NA - 1)
                if first and u == 0:
                    pool.wait_ge(wtab_ready, 1)
                if again:
                    pool.wait_ge(y_done, YB * (UNROLL * g + u - 1))
                nc.gpsimd.tensor_copy(w_now[:, slot, :, :], wtab[:, bass.ds(s, 1), :, :].rearrange("p s h d -> p (s h) d"))\
                  .then_inc(w_staged, 1)
                if first and u == 0:
                    pool.wait_ge(atab_ready, YB)
                if again:
                    pool.wait_ge(r_done, UNROLL * g + u - 1)
                src = atab[:, bass.ds(a, 1), :, :]
                nc.gpsimd.tensor_copy(a_now[:, slot, :, :, :],
                                      src.rearrange("p a k r -> p (a k) r").unsqueeze(2).to_broadcast([P, KT, NQ, QUAD]))\
                  .then_inc(a_staged, 1)
                if first and u == 0:
                    for h in range(HALVES):
                        pool.wait_ge(btab_ready[h], NA)
                if again:
                    pool.wait_ge(z_done, HALVES * (UNROLL * g + u - 1))
                nc.gpsimd.tensor_copy(b_now[:, slot, :], b_tab[:, bass.ds(a, 1), :].rearrange("p a o -> p (a o)"))\
                  .then_inc(b_staged, 1)

            for u in range(UNROLL):
                stage(0, u, True)
            with pool.Fori(1, GROUPS) as g:
                for u in range(UNROLL):
                    stage(g, u, False)

        @block.scalar
        def _(act):
            act.dma_start(b_raw[:, :, :, :].rearrange("p a n r -> p a (n r)"),
                          Bm.rearrange("a (p n) r -> p a (n r)", n=OT)).then_inc(small_landed["b"], 16)
            for a in range(NA):
                act.dma_start(scale[a * RANK:(a + 1) * RANK, :],
                              scalings[a:a + 1].rearrange("(a b) -> a b", a=1).to_broadcast([RANK, 1]))\
                   .then_inc(small_landed["b"], 16)
            act.wait_ge(w0_biased, 1)
            nc.scalar.copy(wtab[:, :, 0, :], w0_raw[:, :, :]).then_inc(wtab_hi, 1)
            act.wait_ge(x_landed[0], 16)
            nc.scalar.copy(x_hi[:, 0, :], x_in[:, 0, :]).then_inc(x_hi_ready, 1)
            for n in range(YB):
                act.wait_ge(at_turned, n + 1)
                nc.scalar.copy(atab[:, :, n * KPB:(n + 1) * KPB, 0:RANK].rearrange("p a k r -> p k a r"),
                               y_ps[:, n, :, :].rearrange("p k (a r) -> p k a r", r=RANK)).then_inc(atab_hi, 1)
            for n in range(MBANKS):
                k, h = n // HALVES, n % HALVES
                if k // KPB == h:
                    act.wait_ge(m_biased, k + 1)
                else:
                    act.wait_ge(w_turned, n + 1)
                nc.scalar.copy(m_hi[:, k, h * BANK:(h + 1) * BANK], m_bank(n)).then_inc(m_hi_ready, 1)
            for n in range(0, NA * HALVES, 2):
                act.wait_ge(b_spread, n + 1)
                a, h = n // HALVES, n % HALVES
                nc.scalar.copy(b_tab[:, a, h * BANK:(h + 1) * BANK], m_bank(n)).then_inc(btab_ready[h], 1)

            def split_x(g, u):
                act.wait_ge(x_landed[u], 16 * g + 16)
                act.wait_ge(y_done, YB * (UNROLL * g + u - 1))
                nc.scalar.copy(x_hi[:, u % 2, :], x_in[:, u, :]).then_inc(x_hi_ready, 1)

            def split_y(g, u, first):
                if not (first and u < 2):
                    act.wait_ge(z_done, HALVES * (UNROLL * g + u - 1))
                for n in range(YB):
                    act.wait_ge(y_done, YB * (UNROLL * g + u) + n + 1)
                    nc.scalar.copy(y_hi[:, u % 2, n * KPB:(n + 1) * KPB, :], y_ps[:, n, :, :]).then_inc(y_hi_ready, 1)

            def split_r(g, u):
                act.wait_ge(r_done, UNROLL * g + u + 1)
                if not (isinstance(g, int) and g == 0 and u == 0):
                    act.wait_ge(z_done, HALVES * (UNROLL * g + u))
                nc.scalar.copy(stack[:, :], r_ps[:, 0:C]).then_inc(r_hi_ready, 1)

            def copy_z(g, u, first):
                act.wait_ge(z_done, HALVES * (UNROLL * g + u) + 1)
                if not first:
                    act.wait_ge(z_stored[u], 16 * g)
                nc.scalar.copy(z_out[:, u, 0:BANK], z_ps[:, u % 2, 0, :]).then_inc(z_copied[0], 1)

            act.wait_ge(x_landed[1], 16)
            nc.scalar.copy(x_hi[:, 1, :], x_in[:, 1, :]).then_inc(x_hi_ready, 1)
            split_y(0, 0, True)

            def step(g, u, first, last):
                split_r(g, u)
                if not (last and u == UNROLL - 1):
                    split_y(g + (u + 1) // UNROLL, (u + 1) % UNROLL, first and u + 1 < UNROLL)
                if not (last and u >= UNROLL - 2):
                    split_x(g + (u + 2) // UNROLL, (u + 2) % UNROLL)
                copy_z(g, u, first)

            for u in range(UNROLL):
                step(0, u, True, False)
            with act.Fori(1, GROUPS - 1) as g:
                for u in range(UNROLL):
                    step(g, u, False, False)
            for u in range(UNROLL):
                step(GROUPS - 1, u, False, True)

        @block.vector
        def _(dve):
            dve.wait_ge(small_landed["w0"], 16)
            dve.wait_ge(ident_ready, 2)
            nc.vector.tensor_tensor(w0_raw[:, :, :], w0_raw[:, :, :],
                                    ident[:, :].unsqueeze(1).to_broadcast([P, NS, D]), ALU.add).then_inc(w0_biased, 1)
            dve.wait_ge(wtab_hi, 1)
            nc.vector.tensor_tensor(wtab[:, :, 1, :], w0_raw[:, :, :], wtab[:, :, 0, :], ALU.subtract)\
              .then_inc(wtab_ready, 1)
            dve.wait_ge(x_hi_ready, 1)
            nc.vector.tensor_tensor(x_lo[:, 0, :], x_in[:, 0, :], x_hi[:, 0, :], ALU.subtract).then_inc(x_lo_ready, 1)
            for n in range(YB):
                dve.wait_ge(atab_hi, n + 1)
                tiles = slice(n * KPB, (n + 1) * KPB)
                nc.vector.tensor_tensor(atab[:, :, tiles, RANK:QUAD].rearrange("p a k r -> p k a r"),
                                        y_ps[:, n, :, :].rearrange("p k (a r) -> p k a r", r=RANK),
                                        atab[:, :, tiles, 0:RANK].rearrange("p a k r -> p k a r"), ALU.subtract)\
                  .then_inc(atab_ready, 1)
            dve.wait_ge(small_landed["b"], 16 * (NA + 1))
            for n in range(HALVES):
                dve.wait_ge(bt_turned, n + 1)
                bank = y_ps[:, n, :, :]
                hi, lo = [t[:, :].rearrange("p (c k) -> p k c", k=OT)[:, n * KPB:(n + 1) * KPB, :] for t in (bt_hi, bt_lo)]
                nc.vector.tensor_scalar(bank, bank, scale[:, 0:1], None, ALU.mult).then_inc(bt_scaled, 1)
                dve.wait_ge(bt_scaled, n + 1)
                nc.vector.tensor_copy(hi, bank).then_inc(bt_split, 1)
                dve.wait_ge(bt_split, 2 * n + 1)
                nc.vector.tensor_tensor(lo, bank, hi, ALU.subtract).then_inc(bt_split, 1)
            def bias_m(n):
                k, h = n // HALVES, n % HALVES
                if k // KPB == h:
                    dve.wait_ge(w_turned, n + 1)
                    tile = m_bank(n)[:, (k % KPB) * P:(k % KPB + 1) * P]
                    nc.vector.tensor_tensor(tile, tile, ident[:, :], ALU.add).then_inc(m_biased, 1)
            bias_m(0)
            for n in range(MBANKS):
                if n + 1 < MBANKS:
                    bias_m(n + 1)
                k, h = n // HALVES, n % HALVES
                cols = slice(h * BANK, (h + 1) * BANK)
                dve.wait_ge(m_hi_ready, n + 1)
                nc.vector.tensor_tensor(m_lo[:, k, cols], m_bank(n), m_hi[:, k, cols], ALU.subtract).then_inc(m_ready, 1)
            for n in range(1, NA * HALVES, 2):
                dve.wait_ge(b_spread, n + 1)
                a, h = n // HALVES, n % HALVES
                nc.vector.tensor_copy(b_tab[:, a, h * BANK:(h + 1) * BANK], m_bank(n)).then_inc(btab_ready[h], 1)

            def split_x(g, u):
                dve.wait_ge(x_hi_ready, UNROLL * g + u + 1)
                nc.vector.tensor_tensor(x_lo[:, u % 2, :], x_in[:, u, :], x_hi[:, u % 2, :], ALU.subtract)\
                  .then_inc(x_lo_ready, 1)

            def split_y(g, u):
                for n in range(YB):
                    dve.wait_ge(y_hi_ready, YB * (UNROLL * g + u) + n + 1)
                    tiles = slice(n * KPB, (n + 1) * KPB)
                    nc.vector.tensor_tensor(y_lo[:, u % 2, tiles, :], y_ps[:, n, :, :], y_hi[:, u % 2, tiles, :],
                                            ALU.subtract).then_inc(y_lo_ready, 1)

            def split_r(g, u):
                dve.wait_ge(r_hi_ready, UNROLL * g + u + 1)
                nc.vector.tensor_tensor(stack[P // 2:P, :], r_ps[P // 2:P, 0:C], stack[P // 2:P, :], ALU.subtract)\
                  .then_inc(stack_ready, 1)

            def copy_z(g, u, first):
                dve.wait_ge(z_done, HALVES * (UNROLL * g + u) + 2)
                if not first:
                    dve.wait_ge(z_stored[u], 16 * g)
                nc.vector.tensor_copy(z_out[:, u, BANK:2 * BANK], z_ps[:, u % 2, 1, :]).then_inc(z_copied[1], 1)

            split_x(0, 1)
            split_y(0, 0)

            def step(g, u, first, last):
                split_r(g, u)
                if not (last and u == UNROLL - 1):
                    split_y(g + (u + 1) // UNROLL, (u + 1) % UNROLL)
                if not (last and u >= UNROLL - 2):
                    split_x(g + (u + 2) // UNROLL, (u + 2) % UNROLL)
                copy_z(g, u, first)

            for u in range(UNROLL):
                step(0, u, True, False)
            with dve.Fori(1, GROUPS - 1) as g:
                for u in range(UNROLL):
                    step(g, u, False, False)
            for u in range(UNROLL):
                step(GROUPS - 1, u, False, True)

        @block.tensor
        def _(pe):
            mm = nc.tensor.matmul

            pe.wait_ge(small_landed["a"], 16)
            pe.wait_ge(ident_ready, 2)
            for k in range(KT):
                turned = nc.tensor.transpose(y_ps[:, k // KPB, k % KPB, :], a_raw[:, k * P:(k + 1) * P], ident[:, :])
                if k % KPB == KPB - 1:
                    turned.then_inc(at_turned, 1)
            pe.wait_ge(b_flat_ready, 1)
            for n in range(OT):
                if n % KPB == 0:
                    pe.wait_ge(atab_ready, n // KPB + 1)
                turned = nc.tensor.transpose(y_ps[:, n // KPB, n % KPB, :],
                                             b_flat[:, n, :, :].rearrange("p a r -> p (a r)"), ident[:, :])
                if n % KPB == KPB - 1:
                    turned.then_inc(bt_turned, 1)
            for n in range(MBANKS):
                k, h = n // HALVES, n % HALVES
                if h == 0:
                    pe.wait_ge(w_landed[k], 16)
                if n >= RING:
                    pe.wait_ge(m_ready, n - RING + 1)
                for j in range(KPB):
                    turned = nc.tensor.transpose(m_bank(n)[:, j * P:(j + 1) * P], w_raw[:, k, h * KPB + j, :], ident[:, :])
                turned.then_inc(w_turned, 1)

            def first_layer(g, u, again):
                slot = u % 2
                pe.wait_ge(w_staged, UNROLL * g + u + 1)
                pe.wait_ge(x_lo_ready, UNROLL * g + u + 1)
                for n in range(YB):
                    if again:
                        pe.wait_ge(y_lo_ready, YB * (UNROLL * g + u - 1) + n + 1)
                    for j in range(KPB):
                        k = n * KPB + j
                        cols = slice(k * P, (k + 1) * P)
                        yt = y_ps[:, n, j, :]
                        mm(yt, x_hi[:, slot, cols], w_now[:, slot, 0, :], start=True, stop=False)
                        mm(yt, x_hi[:, slot, cols], w_now[:, slot, 1, :], start=False, stop=False)
                        done = mm(yt, x_lo[:, slot, cols], w_now[:, slot, 0, :], start=False, stop=True)
                    done.then_inc(y_done, 1)

            def rank_part(g, u, again):
                slot = u % 2
                pe.wait_ge(a_staged, UNROLL * g + u + 1)
                pe.wait_ge(y_lo_ready, YB * (UNROLL * g + u) + YB)
                if again:
                    pe.wait_ge(stack_ready, UNROLL * g + u)
                for k in range(KT):
                    parts = a_now[:, slot, k, :, :].rearrange("p q r -> p (q r)")
                    mm(r_ps[:, 0:C], parts, y_hi[:, slot, k, :], start=(k == 0), stop=False)
                    done = mm(r_ps[:, 0:C], parts, y_lo[:, slot, k, :], start=False, stop=(k == KT - 1))
                done.then_inc(r_done, 1)

            def second_layer(g, u, first):
                slot = u % 2
                for h in range(HALVES):
                    if not (first and u < 2):
                        pe.wait_ge(z_copied[h], UNROLL * g + u - 1)
                    cols = slice(h * BANK, (h + 1) * BANK)
                    z = z_ps[:, slot, h, :]
                    for k in range(KT):
                        mm(z, y_hi[:, slot, k, :], m_hi[:, k, cols], start=(k == 0), stop=False)
                        mm(z, y_hi[:, slot, k, :], m_lo[:, k, cols], start=False, stop=False)
                        mm(z, y_lo[:, slot, k, :], m_hi[:, k, cols], start=False, stop=False)
                    if h == 0:
                        pe.wait_ge(stack_ready, UNROLL * g + u + 1)
                        pe.wait_ge(b_staged, UNROLL * g + u + 1)
                    mm(z, stack[:, :], b_now[:, slot, cols], start=False, stop=True).then_inc(z_done, 1)

            pe.wait_ge(m_ready, MBANKS)
            pe.wait_ge(bt_split, 2 * HALVES)
            pe.wait_ge(sel_ready, 2 * NQ)
            for n in range(NA * HALVES):
                a, h = n // HALVES, n % HALVES
                cols = slice(h * BANK, (h + 1) * BANK)
                if n >= RING:
                    pe.wait_ge(btab_ready[h], (n - RING) // HALVES + 1)
                mm(m_bank(n), sel_hi[:, a, :, :, :].rearrange("p q h r -> p (q h r)"), bt_hi[:, cols], start=True, stop=False)
                mm(m_bank(n), sel_lo[:, a, :, :, :].rearrange("p q h r -> p (q h r)"), bt_lo[:, cols], start=False, stop=True)\
                    .then_inc(b_spread, 1)
            for h in range(HALVES):
                pe.wait_ge(btab_ready[h], NA)
            first_layer(0, 0, False)

            def step(g, u, first, last):
                rank_part(g, u, not (first and u == 0))
                if not (last and u == UNROLL - 1):
                    first_layer(g + (u + 1) // UNROLL, (u + 1) % UNROLL, True)
                second_layer(g, u, first)

            for u in range(UNROLL):
                step(0, u, True, False)
            with pe.Fori(1, GROUPS - 1) as g:
                for u in range(UNROLL):
                    step(g, u, False, False)
            for u in range(UNROLL):
                step(GROUPS - 1, u, False, True)


INPUTS = ["x", "itok_B_0_7", "itok_B_0_6", "L0_cond_weights", "L1_cond_W", "L1_cond_A", "L1_cond_Bm",
          "L1_cond_scalings"]


def kernel(**inputs):
    import numpy as np
    import concourse.bacc as bacc
    from concourse.bass_utils import run_bass_kernel_spmd

    nc = bacc.Bacc("TRN2", target_bir_lowering=False, num_devices=1)
    arrays, args = {}, []
    for name in INPUTS:
        a = np.ascontiguousarray(inputs[name])
        arrays[f"in_{name}"] = a
        args.append(nc.dram_tensor(f"in_{name}", a.shape, mybir.dt.from_np(a.dtype), kind="ExternalInput").ap())
    shape = inputs["x"].shape
    args.append(nc.dram_tensor("out_0", shape, F32, kind="ExternalOutput").ap())
    cond_resid_kernel(nc, *args)
    r = run_bass_kernel_spmd(nc, [arrays], core_ids=[0])
    return r.results[0]["out_0"]
```

```python
from contextlib import ExitStack

import concourse.bass as bass
from concourse import mybir

P = 128
BANK = 512
UNROLL = 4

ALU = mybir.AluOpType
F32 = mybir.dt.float32
F32R = mybir.dt.float32r
I32 = mybir.dt.int32


def cond_resid_kernel(nc, x, subjects, adapters, w0, W, A, Bm, scalings, out):
    NB, C, T = x.shape
    NS, _, D = w0.shape
    O = W.shape[0]
    NA, RANK, _ = A.shape
    KT = T // P
    OT = O // P
    HALVES = O // BANK
    KPB = BANK // P
    TPU = BANK // (2 * C)
    UNITS = KT // TPU
    GROUPS = NB // UNROLL
    QUAD = 2 * RANK
    NQ = P // QUAD
    assert C == D == P and NA * RANK == P and QUAD == 32 and GROUPS >= 3

    with ExitStack() as ctx:
        def sb(name, shape, dt=F32, scope=ctx):
            return scope.enter_context(nc.sbuf_tensor(name, shape, dt))

        def psum(name, shape):
            return ctx.enter_context(nc.psum_tensor(name, shape, F32))

        def sem(name):
            return ctx.enter_context(nc.semaphore(name))

        m_hi = sb("m_hi", [P, KT, O], F32R)
        m_lo = sb("m_lo", [P, KT, O], F32R)
        atab = sb("atab", [P, NA, KT, QUAD], F32R)
        wtab = sb("wtab", [P, NS, 2, D], F32R)
        ident = sb("ident", [P, P])
        ids = sb("ids", [1, 2, NB], I32)
        scale = sb("scale", [P, 1])
        x_in = sb("x_in", [P, UNROLL, T])
        x_hi = sb("x_hi", [P, 2, T], F32R)
        x_lo = sb("x_lo", [P, 2, T], F32R)
        y = sb("y", [P, 2, KT, 2, C], F32R)
        w_now = sb("w_now", [P, 2, 2, D], F32R)
        a_now = sb("a_now", [P, 2, KT, NQ, QUAD], F32R)
        stack = sb("stack", [P, C], F32R)

        with ExitStack() as prep:
            w_raw = sb("w_raw", [P, KT, OT, P], F32, prep)
        b_tab = sb("b_tab", [P, NA, O], F32R)
        with ExitStack() as prep:
            bt_hi = sb("bt_hi", [P, O], F32R, prep)
            bt_lo = sb("bt_lo", [P, O], F32R, prep)
            sel_hi = sb("sel_hi", [P, NA, NQ, 2, RANK], F32R, prep)
            sel_lo = sb("sel_lo", [P, NA, NQ, 2, RANK], F32R, prep)
        z_out = sb("z_out", [P, UNROLL, O])
        with ExitStack() as prep:
            a_raw = sb("a_raw", [P, T], F32, prep)
            w0_raw = sb("w0_raw", [P, NS, D], F32, prep)
        b_now = sb("b_now", [P, 2, O], F32R)
        b_raw = sb("b_raw", [P, NA, OT, RANK])
        b_flat = sb("b_flat", [P, OT, NA, RANK])

        z_ps = psum("z_ps", [P, 2, HALVES, BANK])
        y_ps = psum("y_ps", [P, 2, TPU, 2, C])
        r_ps = psum("r_ps", [P, BANK])

        x_landed = [sem(f"x_landed{u}") for u in range(UNROLL)]
        w_landed = [sem(f"w_landed{k}") for k in range(KT)]
        small_landed = {n: sem(f"{n}_landed") for n in ("ids", "w0", "a", "b")}
        z_stored = [sem(f"z_stored{u}") for u in range(UNROLL)]
        ident_ready = sem("ident_ready")
        w0_biased = sem("w0_biased")
        wtab_hi = sem("wtab_hi")
        wtab_ready = sem("wtab_ready")
        at_turned = sem("at_turned")
        atab_hi = sem("atab_hi")
        atab_ready = sem("atab_ready")
        b_flat_ready = sem("b_flat_ready")
        bt_turned = sem("bt_turned")
        bt_scaled = sem("bt_scaled")
        bt_split = sem("bt_split")
        sel_zeroed = sem("sel_zeroed")
        sel_ready = sem("sel_ready")
        w_turned = sem("w_turned")
        m_biased = sem("m_biased")
        m_hi_ready = sem("m_hi_ready")
        m_ready = sem("m_ready")
        b_spread = sem("b_spread")
        btab_ready = [sem(f"btab_ready{h}") for h in range(HALVES)]
        x_hi_ready = sem("x_hi_ready")
        x_lo_ready = sem("x_lo_ready")
        w_staged = sem("w_staged")
        a_staged = sem("a_staged")
        b_staged = sem("b_staged")
        y_done = sem("y_done")
        y_hi_ready = sem("y_hi_ready")
        y_left = sem("y_left")
        y_lo_ready = sem("y_lo_ready")
        r_done = sem("r_done")
        r_hi_ready = sem("r_hi_ready")
        r_left = sem("r_left")
        stack_ready = sem("stack_ready")
        z_done = sem("z_done")
        z_copied = [sem(f"z_copied{h}") for h in range(HALVES)]

        MBANKS = KT * HALVES
        RING = 2 * HALVES

        def m_bank(n):
            return z_ps[:, (n % RING) // HALVES, n % HALVES, :]

        def y_bank(n):
            return y_ps[:, n, :, :, :].rearrange("p j h c -> p (j h) c")

        block = ctx.enter_context(nc.Block())

        @block.sync
        def _(sp):
            sp.dma_start(w0_raw[:, :, :], w0.rearrange("s c d -> c s d")).then_inc(small_landed["w0"], 16)
            sp.dma_start(x_in[:, 0, :], x[0]).then_inc(x_landed[0], 16)
            sp.dma_start(a_raw[:, :], A.rearrange("a r t -> (a r) t")).then_inc(small_landed["a"], 16)
            for k in range(KT):
                sp.dma_start(w_raw[:, k, :, :],
                             W[:, k * P:(k + 1) * P].rearrange("(n o) t -> o n t", o=P)).then_inc(w_landed[k], 16)
            for b in range(1, UNROLL):
                sp.dma_start(x_in[:, b, :], x[b]).then_inc(x_landed[b], 16)

            def step(g, u, last):
                if not last:
                    sp.wait_ge(x_hi_ready, UNROLL * g + u + 1)
                    sp.wait_ge(x_lo_ready, UNROLL * g + u + 1)
                    sp.dma_start(x_in[:, u, :], x[bass.ds(UNROLL * g + (UNROLL + u), 1), :, :].rearrange("b c t -> (b c) t"))\
                      .then_inc(x_landed[u], 16)
                for h in range(HALVES):
                    sp.wait_ge(z_copied[h], UNROLL * g + u + 1)
                sp.dma_start(out[bass.ds(UNROLL * g + u, 1), :, :].rearrange("b c t -> (b c) t"), z_out[:, u, :])\
                  .then_inc(z_stored[u], 16)

            with sp.Fori(0, GROUPS - 1) as g:
                for u in range(UNROLL):
                    step(g, u, False)
            for u in range(UNROLL):
                step(GROUPS - 1, u, True)
            for u in range(UNROLL):
                sp.wait_ge(z_stored[u], 16 * GROUPS)

        @block.gpsimd
        def _(pool):
            pool.dma_start(ids[0:1, 0, :], subjects.rearrange("(a b) -> a b", a=1)).then_inc(small_landed["ids"], 16)
            pool.dma_start(ids[0:1, 1, :], adapters.rearrange("(a b) -> a b", a=1)).then_inc(small_landed["ids"], 16)
            nc.gpsimd.memset(ident[:, :], 0.0).then_inc(ident_ready, 1)
            pool.wait_ge(ident_ready, 1)
            nc.gpsimd.affine_select(out=ident[:, :], in_=ident[:, :], compare_op=ALU.not_equal, fill=1.0,
                                    base=0, pattern=[[-1, P]], channel_multiplier=1).then_inc(ident_ready, 1)
            nc.gpsimd.memset(sel_hi[:, :, :, :, :].bitcast(F32), 0.0).then_inc(sel_zeroed, 1)
            nc.gpsimd.memset(sel_lo[:, :, :, :, :].bitcast(F32), 0.0).then_inc(sel_zeroed, 1)
            pool.wait_ge(ident_ready, 2)
            pool.wait_ge(sel_zeroed, 2)
            for q in range(NQ):
                sel = sel_hi if q % 2 == 0 else sel_lo
                for half in range(2):
                    nc.gpsimd.tensor_copy(sel[:, :, q, half, :],
                                          ident[:, :].rearrange("p (a r) -> p a r", r=RANK)).then_inc(sel_ready, 1)
            pool.wait_ge(small_landed["b"], 16 * (NA + 1))
            nc.gpsimd.tensor_copy(b_flat[:, :, :, :], b_raw[:, :, :, :].rearrange("p a n r -> p n a r"))\
              .then_inc(b_flat_ready, 1)
            pool.wait_ge(small_landed["ids"], 32)

            def stage(g, u, first):
                slot = u % 2
                again = not (first and u < 2)
                s = pool.value_load(ids[0:1, 0, bass.ds(UNROLL * g + u, 1)], min_val=0, max_val=NS - 1)
                a = pool.value_load(ids[0:1, 1, bass.ds(UNROLL * g + u, 1)], min_val=0, max_val=NA - 1)
                if first and u == 0:
                    pool.wait_ge(wtab_ready, 1)
                if again:
                    pool.wait_ge(y_done, UNITS * (UNROLL * g + u - 1))
                nc.gpsimd.tensor_copy(w_now[:, slot, :, :], wtab[:, bass.ds(s, 1), :, :].rearrange("p s h d -> p (s h) d"))\
                  .then_inc(w_staged, 1)
                if first and u == 0:
                    for h in range(HALVES):
                        pool.wait_ge(btab_ready[h], NA)
                if again:
                    pool.wait_ge(z_done, HALVES * (UNROLL * g + u - 1))
                nc.gpsimd.tensor_copy(b_now[:, slot, :], b_tab[:, bass.ds(a, 1), :].rearrange("p a o -> p (a o)"))\
                  .then_inc(b_staged, 1)

            for u in range(UNROLL):
                stage(0, u, True)
            with pool.Fori(1, GROUPS) as g:
                for u in range(UNROLL):
                    stage(g, u, False)

        @block.scalar
        def _(act):
            act.dma_start(b_raw[:, :, :, :].rearrange("p a n r -> p a (n r)"),
                          Bm.rearrange("a (p n) r -> p a (n r)", n=OT)).then_inc(small_landed["b"], 16)
            for a in range(NA):
                act.dma_start(scale[a * RANK:(a + 1) * RANK, :],
                              scalings[a:a + 1].rearrange("(a b) -> a b", a=1).to_broadcast([RANK, 1]))\
                   .then_inc(small_landed["b"], 16)
            act.wait_ge(w0_biased, 1)
            nc.scalar.copy(wtab[:, :, 0, :], w0_raw[:, :, :]).then_inc(wtab_hi, 1)
            act.wait_ge(x_landed[0], 16)
            nc.scalar.copy(x_hi[:, 0, :], x_in[:, 0, :]).then_inc(x_hi_ready, 1)
            for n in range(KT // KPB):
                act.wait_ge(at_turned, n + 1)
                nc.scalar.copy(atab[:, :, n * KPB:(n + 1) * KPB, 0:RANK].rearrange("p a k r -> p k a r"),
                               y_bank(n).rearrange("p k (a r) -> p k a r", r=RANK)).then_inc(atab_hi, 1)
            for n in range(MBANKS):
                k, h = n // HALVES, n % HALVES
                if k // KPB == h:
                    act.wait_ge(m_biased, k + 1)
                else:
                    act.wait_ge(w_turned, n + 1)
                nc.scalar.copy(m_hi[:, k, h * BANK:(h + 1) * BANK], m_bank(n)).then_inc(m_hi_ready, 1)
            for n in range(0, NA * HALVES, 2):
                act.wait_ge(b_spread, n + 1)
                a, h = n // HALVES, n % HALVES
                nc.scalar.copy(b_tab[:, a, h * BANK:(h + 1) * BANK], m_bank(n)).then_inc(btab_ready[h], 1)

            def split_x(g, u, first):
                act.wait_ge(x_landed[u], 16 * g + 16)
                if not (first and u < 2):
                    act.wait_ge(y_done, UNITS * (UNROLL * g + u - 1))
                nc.scalar.copy(x_hi[:, u % 2, :], x_in[:, u, :]).then_inc(x_hi_ready, 1)

            def stage_a(g, u, first):
                a = act.value_load(ids[0:1, 1, bass.ds(UNROLL * g + u, 1)], min_val=0, max_val=NA - 1)
                if not (first and u < 2):
                    act.wait_ge(r_done, UNROLL * g + u - 1)
                parts = atab[:, bass.ds(a, 1), :, :].rearrange("p a k r -> p (a k) r")
                nc.scalar.copy(a_now[:, u % 2, :, :, :], parts.unsqueeze(2).to_broadcast([P, KT, NQ, QUAD]))\
                  .then_inc(a_staged, 1)

            def split_y(g, u, n, first):
                if n == 0 and not (first and u < 2):
                    act.wait_ge(z_done, HALVES * (UNROLL * g + u - 1))
                act.wait_ge(y_done, UNITS * (UNROLL * g + u) + n + 1)
                tiles = slice(n * TPU, (n + 1) * TPU)
                nc.scalar.copy(y[:, u % 2, tiles, 0, :], y_ps[:, n % 2, :, 0, :]).then_inc(y_hi_ready, 1)

            def split_r(g, u, first):
                act.wait_ge(r_done, UNROLL * g + u + 1)
                if not (first and u == 0):
                    act.wait_ge(z_done, HALVES * (UNROLL * g + u))
                nc.scalar.copy(stack[:, :], r_ps[:, 0:C]).then_inc(r_hi_ready, 1)

            def copy_z(g, u, first):
                act.wait_ge(z_done, HALVES * (UNROLL * g + u) + 1)
                if not first:
                    act.wait_ge(z_stored[u], 16 * g)
                nc.scalar.copy(z_out[:, u, 0:BANK], z_ps[:, u % 2, 0, :]).then_inc(z_copied[0], 1)

            act.wait_ge(small_landed["ids"], 32)
            act.wait_ge(atab_ready, KT // KPB)
            stage_a(0, 0, True)
            split_x(0, 1, True)
            for n in range(UNITS):
                split_y(0, 0, n, True)

            def step(g, u, first, last):
                g1, u1, first1 = g + (u + 1) // UNROLL, (u + 1) % UNROLL, first and u + 1 < UNROLL
                g2, u2 = g + (u + 2) // UNROLL, (u + 2) % UNROLL
                next1, next2 = not (last and u == UNROLL - 1), not (last and u >= UNROLL - 2)
                split_r(g, u, first)
                if next1:
                    split_y(g1, u1, 0, first1)
                if next2:
                    split_x(g2, u2, False)
                if next1:
                    split_y(g1, u1, 1, first1)
                    stage_a(g1, u1, first1)
                copy_z(g, u, first)
                if next1:
                    split_y(g1, u1, 2, first1)
                    split_y(g1, u1, 3, first1)

            for u in range(UNROLL):
                step(0, u, True, False)
            with act.Fori(1, GROUPS - 1) as g:
                for u in range(UNROLL):
                    step(g, u, False, False)
            for u in range(UNROLL):
                step(GROUPS - 1, u, False, True)

        @block.vector
        def _(dve):
            dve.wait_ge(small_landed["w0"], 16)
            dve.wait_ge(ident_ready, 2)
            nc.vector.tensor_tensor(w0_raw[:, :, :], w0_raw[:, :, :],
                                    ident[:, :].unsqueeze(1).to_broadcast([P, NS, D]), ALU.add).then_inc(w0_biased, 1)
            dve.wait_ge(wtab_hi, 1)
            nc.vector.tensor_tensor(wtab[:, :, 1, :], w0_raw[:, :, :], wtab[:, :, 0, :], ALU.subtract)\
              .then_inc(wtab_ready, 1)
            dve.wait_ge(x_hi_ready, 1)
            nc.vector.tensor_tensor(x_lo[:, 0, :], x_in[:, 0, :], x_hi[:, 0, :], ALU.subtract).then_inc(x_lo_ready, 1)
            for n in range(KT // KPB):
                dve.wait_ge(atab_hi, n + 1)
                tiles = slice(n * KPB, (n + 1) * KPB)
                nc.vector.tensor_tensor(atab[:, :, tiles, RANK:QUAD].rearrange("p a k r -> p k a r"),
                                        y_bank(n).rearrange("p k (a r) -> p k a r", r=RANK),
                                        atab[:, :, tiles, 0:RANK].rearrange("p a k r -> p k a r"), ALU.subtract)\
                  .then_inc(atab_ready, 1)
            dve.wait_ge(small_landed["b"], 16 * (NA + 1))
            for n in range(HALVES):
                dve.wait_ge(bt_turned, n + 1)
                bank = y_bank(n)
                hi, lo = [t[:, :].rearrange("p (c k) -> p k c", k=OT)[:, n * KPB:(n + 1) * KPB, :] for t in (bt_hi, bt_lo)]
                nc.vector.tensor_scalar(bank, bank, scale[:, 0:1], None, ALU.mult).then_inc(bt_scaled, 1)
                dve.wait_ge(bt_scaled, n + 1)
                nc.vector.tensor_copy(hi, bank).then_inc(bt_split, 1)
                dve.wait_ge(bt_split, 2 * n + 1)
                nc.vector.tensor_tensor(lo, bank, hi, ALU.subtract).then_inc(bt_split, 1)
            def bias_m(n):
                k, h = n // HALVES, n % HALVES
                if k // KPB == h:
                    dve.wait_ge(w_turned, n + 1)
                    tile = m_bank(n)[:, (k % KPB) * P:(k % KPB + 1) * P]
                    nc.vector.tensor_tensor(tile, tile, ident[:, :], ALU.add).then_inc(m_biased, 1)
            bias_m(0)
            for n in range(MBANKS):
                if n + 1 < MBANKS:
                    bias_m(n + 1)
                k, h = n // HALVES, n % HALVES
                cols = slice(h * BANK, (h + 1) * BANK)
                dve.wait_ge(m_hi_ready, n + 1)
                nc.vector.tensor_tensor(m_lo[:, k, cols], m_bank(n), m_hi[:, k, cols], ALU.subtract).then_inc(m_ready, 1)
            for n in range(1, NA * HALVES, 2):
                dve.wait_ge(b_spread, n + 1)
                a, h = n // HALVES, n % HALVES
                nc.vector.tensor_copy(b_tab[:, a, h * BANK:(h + 1) * BANK], m_bank(n)).then_inc(btab_ready[h], 1)

            def split_x(g, u):
                dve.wait_ge(x_hi_ready, UNROLL * g + u + 1)
                nc.vector.tensor_tensor(x_lo[:, u % 2, :], x_in[:, u, :], x_hi[:, u % 2, :], ALU.subtract)\
                  .then_inc(x_lo_ready, 1)

            def split_y(g, u, n):
                unit = UNITS * (UNROLL * g + u) + n
                tiles = slice(n * TPU, (n + 1) * TPU)
                hi, lo = y[:, u % 2, tiles, 0, :], y[:, u % 2, tiles, 1, :]
                dve.wait_ge(y_hi_ready, unit + 1)
                nc.vector.tensor_tensor(lo, y_ps[:, n % 2, :, 0, :], hi, ALU.subtract).then_inc(y_left, 1)
                dve.wait_ge(y_left, unit + 1)
                nc.vector.tensor_tensor(lo, y_ps[:, n % 2, :, 1, :], lo, ALU.add).then_inc(y_lo_ready, 1)

            def split_r(g, u):
                lo = stack[P // 2:P, :]
                dve.wait_ge(r_hi_ready, UNROLL * g + u + 1)
                nc.vector.tensor_tensor(lo, r_ps[P // 2:P, 0:C], lo, ALU.subtract).then_inc(r_left, 1)
                dve.wait_ge(r_left, UNROLL * g + u + 1)
                nc.vector.tensor_tensor(lo, r_ps[P // 2:P, C:2 * C], lo, ALU.add).then_inc(stack_ready, 1)

            def copy_z(g, u, first):
                dve.wait_ge(z_done, HALVES * (UNROLL * g + u) + 2)
                if not first:
                    dve.wait_ge(z_stored[u], 16 * g)
                nc.vector.tensor_copy(z_out[:, u, BANK:2 * BANK], z_ps[:, u % 2, 1, :]).then_inc(z_copied[1], 1)

            split_x(0, 1)
            for n in range(UNITS):
                split_y(0, 0, n)

            def step(g, u, first, last):
                g1, u1 = g + (u + 1) // UNROLL, (u + 1) % UNROLL
                g2, u2 = g + (u + 2) // UNROLL, (u + 2) % UNROLL
                next1, next2 = not (last and u == UNROLL - 1), not (last and u >= UNROLL - 2)
                split_r(g, u)
                for n in range(UNITS if next1 else 0):
                    split_y(g1, u1, n)
                    if n == 0 and next2:
                        split_x(g2, u2)
                copy_z(g, u, first)

            for u in range(UNROLL):
                step(0, u, True, False)
            with dve.Fori(1, GROUPS - 1) as g:
                for u in range(UNROLL):
                    step(g, u, False, False)
            for u in range(UNROLL):
                step(GROUPS - 1, u, False, True)

        @block.tensor
        def _(pe):
            mm = nc.tensor.matmul

            pe.wait_ge(small_landed["a"], 16)
            pe.wait_ge(ident_ready, 2)
            for k in range(KT):
                turned = nc.tensor.transpose(y_bank(k // KPB)[:, k % KPB, :], a_raw[:, k * P:(k + 1) * P], ident[:, :])
                if k % KPB == KPB - 1:
                    turned.then_inc(at_turned, 1)
            pe.wait_ge(b_flat_ready, 1)
            for n in range(OT):
                if n % KPB == 0:
                    pe.wait_ge(atab_ready, n // KPB + 1)
                turned = nc.tensor.transpose(y_bank(n // KPB)[:, n % KPB, :],
                                             b_flat[:, n, :, :].rearrange("p a r -> p (a r)"), ident[:, :])
                if n % KPB == KPB - 1:
                    turned.then_inc(bt_turned, 1)
            for n in range(MBANKS):
                k, h = n // HALVES, n % HALVES
                if h == 0:
                    pe.wait_ge(w_landed[k], 16)
                if n >= RING:
                    pe.wait_ge(m_ready, n - RING + 1)
                for j in range(KPB):
                    turned = nc.tensor.transpose(m_bank(n)[:, j * P:(j + 1) * P], w_raw[:, k, h * KPB + j, :], ident[:, :])
                turned.then_inc(w_turned, 1)

            def first_layer(g, u, n, first):
                slot = u % 2
                if n == 0:
                    pe.wait_ge(w_staged, UNROLL * g + u + 1)
                    pe.wait_ge(x_lo_ready, UNROLL * g + u + 1)
                if not (first and u == 0 and n < 2):
                    pe.wait_ge(y_lo_ready, UNITS * (UNROLL * g + u) + n - 1)
                both = w_now[:, slot, :, :].rearrange("p h d -> p (h d)")
                for j in range(TPU):
                    k = n * TPU + j
                    cols = slice(k * P, (k + 1) * P)
                    yt = y_ps[:, n % 2, j, :, :].rearrange("p h c -> p (h c)")
                    mm(yt, x_hi[:, slot, cols], both, start=True, stop=False)
                    done = mm(yt, x_lo[:, slot, cols], both, start=False, stop=True)
                done.then_inc(y_done, 1)

            def rank_part(g, u, first):
                slot = u % 2
                pe.wait_ge(a_staged, UNROLL * g + u + 1)
                pe.wait_ge(y_lo_ready, UNITS * (UNROLL * g + u) + UNITS)
                if not (first and u == 0):
                    pe.wait_ge(stack_ready, UNROLL * g + u)
                for k in range(KT):
                    done = mm(r_ps[:, 0:2 * C], a_now[:, slot, k, :, :].rearrange("p q r -> p (q r)"),
                              y[:, slot, k, :, :].rearrange("p h c -> p (h c)"), start=(k == 0), stop=(k == KT - 1))
                done.then_inc(r_done, 1)

            def second_layer(g, u, h, ks, first):
                slot = u % 2
                if 0 in ks and not (first and u < 2):
                    pe.wait_ge(z_copied[h], UNROLL * g + u - 1)
                cols = slice(h * BANK, (h + 1) * BANK)
                z = z_ps[:, slot, h, :]
                for k in ks:
                    mm(z, y[:, slot, k, 0, :], m_hi[:, k, cols], start=(k == 0), stop=False)
                    mm(z, y[:, slot, k, 0, :], m_lo[:, k, cols], start=False, stop=False)
                    mm(z, y[:, slot, k, 1, :], m_hi[:, k, cols], start=False, stop=False)

            def add_rank_part(g, u, h):
                if h == 0:
                    pe.wait_ge(stack_ready, UNROLL * g + u + 1)
                    pe.wait_ge(b_staged, UNROLL * g + u + 1)
                mm(z_ps[:, u % 2, h, :], stack[:, :], b_now[:, u % 2, h * BANK:(h + 1) * BANK], start=False, stop=True)\
                    .then_inc(z_done, 1)

            pe.wait_ge(m_ready, MBANKS)
            pe.wait_ge(bt_split, 2 * HALVES)
            pe.wait_ge(sel_ready, 2 * NQ)
            for n in range(NA * HALVES):
                a, h = n // HALVES, n % HALVES
                cols = slice(h * BANK, (h + 1) * BANK)
                if n >= RING:
                    pe.wait_ge(btab_ready[h], (n - RING) // HALVES + 1)
                mm(m_bank(n), sel_hi[:, a, :, :, :].rearrange("p q h r -> p (q h r)"), bt_hi[:, cols], start=True, stop=False)
                mm(m_bank(n), sel_lo[:, a, :, :, :].rearrange("p q h r -> p (q h r)"), bt_lo[:, cols], start=False, stop=True)\
                    .then_inc(b_spread, 1)
            for h in range(HALVES):
                pe.wait_ge(btab_ready[h], NA)
            for n in range(UNITS):
                first_layer(0, 0, n, True)

            def step(g, u, first, last):
                g1, u1, first1 = g + (u + 1) // UNROLL, (u + 1) % UNROLL, first and u + 1 < UNROLL
                rank_part(g, u, first)
                for n in range(UNITS):
                    if not (last and u == UNROLL - 1):
                        first_layer(g1, u1, n, first1)
                    h, part = n * HALVES // UNITS, n % (UNITS // HALVES)
                    tiles = KT * HALVES // UNITS
                    second_layer(g, u, h, range(part * tiles, (part + 1) * tiles), first)
                    if (part + 1) * tiles == KT:
                        add_rank_part(g, u, h)

            for u in range(UNROLL):
                step(0, u, True, False)
            with pe.Fori(1, GROUPS - 1) as g:
                for u in range(UNROLL):
                    step(g, u, False, False)
            for u in range(UNROLL):
                step(GROUPS - 1, u, False, True)


INPUTS = ["x", "itok_B_0_7", "itok_B_0_6", "L0_cond_weights", "L1_cond_W", "L1_cond_A", "L1_cond_Bm",
          "L1_cond_scalings"]


def kernel(**inputs):
    import numpy as np
    import concourse.bacc as bacc
    from concourse.bass_utils import run_bass_kernel_spmd

    nc = bacc.Bacc("TRN2", target_bir_lowering=False, num_devices=1)
    arrays, args = {}, []
    for name in INPUTS:
        a = np.ascontiguousarray(inputs[name])
        arrays[f"in_{name}"] = a
        args.append(nc.dram_tensor(f"in_{name}", a.shape, mybir.dt.from_np(a.dtype), kind="ExternalInput").ap())
    shape = inputs["x"].shape
    args.append(nc.dram_tensor("out_0", shape, F32, kind="ExternalOutput").ap())
    cond_resid_kernel(nc, *args)
    r = run_bass_kernel_spmd(nc, [arrays], core_ids=[0])
    return r.results[0]["out_0"]
```

```python
from contextlib import ExitStack

import concourse.bass as bass
from concourse import mybir

P = 128
BANK = 512
UNROLL = 4

ALU = mybir.AluOpType
F32 = mybir.dt.float32
F32R = mybir.dt.float32r
I32 = mybir.dt.int32


def cond_resid_kernel(nc, x, subjects, adapters, w0, W, A, Bm, scalings, out):
    NB, C, T = x.shape
    NS, _, D = w0.shape
    O = W.shape[0]
    NA, RANK, _ = A.shape
    KT = T // P
    OT = O // P
    HALVES = O // BANK
    KPB = BANK // P
    TPU = BANK // (2 * C)
    UNITS = KT // TPU
    GROUPS = NB // UNROLL
    QUAD = 2 * RANK
    NQ = P // QUAD
    PIECES = 3
    PW = (QUAD + O) // PIECES
    assert PIECES * PW == QUAD + O and PW % 2 == 0 and PW + C <= BANK
    assert C == D == P and UNITS == 4 and HALVES == 2 and NA * RANK == P and QUAD == 32 and GROUPS >= 3

    with ExitStack() as ctx:
        def sb(name, shape, dt=F32, scope=ctx):
            return scope.enter_context(nc.sbuf_tensor(name, shape, dt))

        def psum(name, shape):
            return ctx.enter_context(nc.psum_tensor(name, shape, F32))

        def sem(name):
            return ctx.enter_context(nc.semaphore(name))

        m_hi = sb("m_hi", [P, KT, QUAD + O], F32R)
        m_lo = sb("m_lo", [P, KT, O], F32R)
        atab = sb("atab", [P, NA, KT, QUAD], F32R)
        wtab = sb("wtab", [P, NS, 2, D], F32R)
        ident = sb("ident", [P, P])
        ident_r = sb("ident_r", [P, P], F32R)
        ids = sb("ids", [1, 2, NB], I32)
        scale = sb("scale", [P, 1])
        x_in = sb("x_in", [P, UNROLL, T])
        x_hi = sb("x_hi", [P, 2, T], F32R)
        x_lo = sb("x_lo", [P, 2, T], F32R)
        y = sb("y", [P, 2, KT, 2, C], F32R)
        w_now = sb("w_now", [P, 2, 2, D], F32R)
        r_parts = sb("r_parts", [P, NQ, QUAD], F32R)
        stack = sb("stack", [P, C], F32R)

        with ExitStack() as prep:
            w_raw = sb("w_raw", [P, KT, OT, P], F32, prep)
        b_tab = sb("b_tab", [P, NA, O], F32R)
        with ExitStack() as prep:
            bt_hi = sb("bt_hi", [P, O], F32R, prep)
            bt_lo = sb("bt_lo", [P, O], F32R, prep)
            sel_hi = sb("sel_hi", [P, NA, NQ, 2, RANK], F32R, prep)
            sel_lo = sb("sel_lo", [P, NA, NQ, 2, RANK], F32R, prep)
        z_out = sb("z_out", [P, UNROLL, O])
        with ExitStack() as prep:
            a_raw = sb("a_raw", [P, T], F32, prep)
            w0_raw = sb("w0_raw", [P, NS, D], F32, prep)
        b_now = sb("b_now", [P, 2, O], F32R)
        b_raw = sb("b_raw", [P, NA, OT, RANK])
        b_flat = sb("b_flat", [P, OT, NA, RANK])

        z_ps = psum("z_ps", [P, 2, PIECES, BANK])
        y_ps = psum("y_ps", [P, 2, TPU, 2, C])

        x_landed = [sem(f"x_landed{u}") for u in range(UNROLL)]
        w_landed = [sem(f"w_landed{k}") for k in range(KT)]
        small_landed = {n: sem(f"{n}_landed") for n in ("ids", "w0", "a", "b", "scale")}
        z_stored = [sem(f"z_stored{u}") for u in range(UNROLL)]
        ident_ready = sem("ident_ready")
        ident_r_ready = sem("ident_r_ready")
        w0_biased = sem("w0_biased")
        wtab_hi = sem("wtab_hi")
        wtab_ready = sem("wtab_ready")
        at_turned = sem("at_turned")
        atab_hi = sem("atab_hi")
        atab_ready = sem("atab_ready")
        b_flat_ready = sem("b_flat_ready")
        bt_turned = sem("bt_turned")
        bt_scaled = sem("bt_scaled")
        bt_split = sem("bt_split")
        sel_zeroed = sem("sel_zeroed")
        sel_ready = sem("sel_ready")
        w_turned = sem("w_turned")
        m_biased = sem("m_biased")
        m_hi_ready = sem("m_hi_ready")
        m_ready = sem("m_ready")
        b_spread = sem("b_spread")
        btab_ready = [sem(f"btab_ready{h}") for h in range(HALVES)]
        x_hi_ready = sem("x_hi_ready")
        x_lo_ready = sem("x_lo_ready")
        w_staged = sem("w_staged")
        a_staged = sem("a_staged")
        b_staged = sem("b_staged")
        y_done = sem("y_done")
        y_hi_ready = sem("y_hi_ready")
        y_left = sem("y_left")
        y_lo_ready = sem("y_lo_ready")
        piece_done = sem("piece_done")
        r_hi_ready = sem("r_hi_ready")
        r_lo_ready = sem("r_lo_ready")
        r_turned = sem("r_turned")
        stack_ready = sem("stack_ready")
        z_done = sem("z_done")
        z_copied = [sem(f"z_copied{i}") for i in range(PIECES)]

        MBANKS = KT * HALVES
        RING = 2 * HALVES

        def m_bank(n):
            return z_ps[:, (n % RING) // HALVES, n % HALVES, :]

        def turn_bank(n):
            return z_ps[:, 1, n, :].rearrange("p (k c) -> p k c", c=P)

        def spread_bank(n):
            return z_ps[:, 1, n % HALVES, :]

        def piece(i):
            start = PW * i - QUAD
            return (slice(0, PW - QUAD), slice(QUAD, PW)) if i == 0 else (slice(start, start + PW), slice(0, PW))

        def r_turn_bank(slot):
            return z_ps[:, slot, 0, PW:PW + C]

        block = ctx.enter_context(nc.Block())

        @block.sync
        def _(sp):
            for k in range(KT):
                sp.dma_start(w_raw[:, k, :, :],
                             W[:, k * P:(k + 1) * P].rearrange("(n o) t -> o n t", o=P)).then_inc(w_landed[k], 16)
                if k == KT // 2:
                    sp.dma_start(w0_raw[:, :, :], w0.rearrange("s c d -> c s d")).then_inc(small_landed["w0"], 16)
            sp.dma_start(x_in[:, 0, :], x[0]).then_inc(x_landed[0], 16)
            sp.dma_start(a_raw[:, :], A.rearrange("a r t -> (a r) t")).then_inc(small_landed["a"], 16)
            sp.dma_start(b_raw[:, :, :, :].rearrange("p a n r -> p a (n r)"),
                         Bm.rearrange("a (p n) r -> p a (n r)", n=OT)).then_inc(small_landed["b"], 16)
            sp.dma_start(x_in[:, 1, :], x[1]).then_inc(x_landed[1], 16)
            for a in range(NA):
                sp.dma_start(scale[a * RANK:(a + 1) * RANK, :],
                             scalings[a:a + 1].rearrange("(a b) -> a b", a=1).to_broadcast([RANK, 1]))\
                  .then_inc(small_landed["scale"], 16)
            for b in range(2, UNROLL):
                sp.dma_start(x_in[:, b, :], x[b]).then_inc(x_landed[b], 16)


            def step(g, u, last):
                if not last:
                    sp.wait_ge(x_hi_ready, UNROLL * g + u + 1)
                    sp.wait_ge(x_lo_ready, UNROLL * g + u + 1)
                    sp.dma_start(x_in[:, u, :], x[bass.ds(UNROLL * g + (UNROLL + u), 1), :, :].rearrange("b c t -> (b c) t"))\
                      .then_inc(x_landed[u], 16)
                for i in range(PIECES):
                    sp.wait_ge(z_copied[i], UNROLL * g + u + 1)
                sp.dma_start(out[bass.ds(UNROLL * g + u, 1), :, :].rearrange("b c t -> (b c) t"), z_out[:, u, :])\
                  .then_inc(z_stored[u], 16)

            with sp.Fori(0, GROUPS - 1) as g:
                for u in range(UNROLL):
                    step(g, u, False)
            for u in range(UNROLL):
                step(GROUPS - 1, u, True)
            for u in range(UNROLL):
                sp.wait_ge(z_stored[u], 16 * GROUPS)

        @block.gpsimd
        def _(pool):
            pool.dma_start(ids[0:1, 0, :], subjects.rearrange("(a b) -> a b", a=1)).then_inc(small_landed["ids"], 16)
            pool.dma_start(ids[0:1, 1, :], adapters.rearrange("(a b) -> a b", a=1)).then_inc(small_landed["ids"], 16)
            nc.gpsimd.memset(ident[:, :], 0.0).then_inc(ident_ready, 1)
            pool.wait_ge(ident_ready, 1)
            nc.gpsimd.affine_select(out=ident[:, :], in_=ident[:, :], compare_op=ALU.not_equal, fill=1.0,
                                    base=0, pattern=[[-1, P]], channel_multiplier=1).then_inc(ident_ready, 1)
            nc.gpsimd.memset(sel_hi[:, :, :, :, :].bitcast(F32), 0.0).then_inc(sel_zeroed, 1)
            nc.gpsimd.memset(sel_lo[:, :, :, :, :].bitcast(F32), 0.0).then_inc(sel_zeroed, 1)
            pool.wait_ge(ident_ready, 2)
            pool.wait_ge(sel_zeroed, 2)
            for q in range(NQ):
                sel = sel_hi if q % 2 == 0 else sel_lo
                for half in range(2):
                    nc.gpsimd.tensor_copy(sel[:, :, q, half, :],
                                          ident[:, :].rearrange("p (a r) -> p a r", r=RANK)).then_inc(sel_ready, 1)
            pool.wait_ge(small_landed["w0"], 16)
            nc.gpsimd.tensor_tensor(w0_raw[:, :, :], w0_raw[:, :, :],
                                    ident[:, :].unsqueeze(1).to_broadcast([P, NS, D]), ALU.add).then_inc(w0_biased, 1)
            pool.wait_ge(wtab_hi, 1)
            nc.gpsimd.tensor_tensor(wtab[:, :, 1, :], w0_raw[:, :, :], wtab[:, :, 0, :], ALU.subtract)\
              .then_inc(wtab_ready, 1)
            pool.wait_ge(small_landed["ids"], 32)

            def stage_w(g, u, first):
                s = pool.value_load(ids[0:1, 0, bass.ds(UNROLL * g + u, 1)], min_val=0, max_val=NS - 1)
                if not (first and u < 2):
                    pool.wait_ge(y_done, UNITS * (UNROLL * g + u - 1))
                nc.gpsimd.tensor_copy(w_now[:, u % 2, :, :], wtab[:, bass.ds(s, 1), :, :].rearrange("p s h d -> p (s h) d"))\
                  .then_inc(w_staged, 1)

            def stage_b(g, u, first):
                a = pool.value_load(ids[0:1, 1, bass.ds(UNROLL * g + u, 1)], min_val=0, max_val=NA - 1)
                if first and u == 0:
                    for h in range(HALVES):
                        pool.wait_ge(btab_ready[h], NA)
                if not (first and u < 2):
                    pool.wait_ge(z_done, PIECES * (UNROLL * g + u - 1))
                nc.gpsimd.tensor_copy(b_now[:, u % 2, :], b_tab[:, bass.ds(a, 1), :].rearrange("p a o -> p (a o)"))\
                  .then_inc(b_staged, 1)

            def step(g, u, first, last):
                if not (last and u == UNROLL - 1):
                    stage_w(g + (u + 1) // UNROLL, (u + 1) % UNROLL, first and u + 1 < UNROLL)
                stage_b(g, u, first)

            pool.wait_ge(wtab_ready, 1)
            stage_w(0, 0, True)
            for u in range(UNROLL):
                step(0, u, True, False)
            with pool.Fori(1, GROUPS - 1) as g:
                for u in range(UNROLL):
                    step(g, u, False, False)
            for u in range(UNROLL):
                step(GROUPS - 1, u, False, True)

        @block.scalar
        def _(act):
            act.wait_ge(ident_ready, 2)
            nc.scalar.copy(ident_r[:, :], ident[:, :]).then_inc(ident_r_ready, 1)
            for n in range(MBANKS):
                k, h = n // HALVES, n % HALVES
                if k // KPB == h:
                    act.wait_ge(m_biased, k + 1)
                else:
                    act.wait_ge(w_turned, n + 1)
                nc.scalar.copy(m_hi[:, k, QUAD + h * BANK:QUAD + (h + 1) * BANK], m_bank(n)).then_inc(m_hi_ready, 1)
                if n == MBANKS // 2:
                    act.wait_ge(w0_biased, 1)
                    nc.scalar.copy(wtab[:, :, 0, :], w0_raw[:, :, :]).then_inc(wtab_hi, 1)
                if n == MBANKS * 3 // 4:
                    act.wait_ge(x_landed[0], 16)
                    nc.scalar.copy(x_hi[:, 0, :], x_in[:, 0, :]).then_inc(x_hi_ready, 1)

            def split_x(g, u, first):
                act.wait_ge(x_landed[u], 16 * g + 16)
                if not (first and u < 2):
                    act.wait_ge(y_done, UNITS * (UNROLL * g + u - 1))
                nc.scalar.copy(x_hi[:, u % 2, :], x_in[:, u, :]).then_inc(x_hi_ready, 1)

            def stage_a(g, u, first):
                a = act.value_load(ids[0:1, 1, bass.ds(UNROLL * g + u, 1)], min_val=0, max_val=NA - 1)
                if not (first and u == 0):
                    act.wait_ge(piece_done, UNROLL * g + u)
                nc.scalar.copy(m_hi[:, :, 0:QUAD], atab[:, bass.ds(a, 1), :, :].rearrange("p a k r -> p (a k) r"))\
                  .then_inc(a_staged, 1)

            def split_y(g, u, n, first):
                if n == 0 and not (first and u < 2):
                    act.wait_ge(z_done, PIECES * (UNROLL * g + u - 1))
                act.wait_ge(y_done, UNITS * (UNROLL * g + u) + n + 1)
                tiles = slice(n * TPU, (n + 1) * TPU)
                nc.scalar.copy(y[:, u % 2, tiles, 0, :], y_ps[:, n % 2, :, 0, :]).then_inc(y_hi_ready, 1)

            def split_r(g, u, first):
                act.wait_ge(piece_done, UNROLL * g + u + 1)
                if not (first and u == 0):
                    act.wait_ge(r_turned, UNROLL * g + u)
                nc.scalar.copy(r_parts[:, 0:NQ // 2, :],
                               z_ps[:, u % 2, 0, 0:QUAD].unsqueeze(1).to_broadcast([P, NQ // 2, QUAD])).then_inc(r_hi_ready, 1)

            def fill_stack(g, u, first):
                act.wait_ge(r_turned, UNROLL * g + u + 1)
                if not (first and u == 0):
                    act.wait_ge(z_done, PIECES * (UNROLL * g + u))
                nc.scalar.copy(stack[:, :], r_turn_bank(u % 2)).then_inc(stack_ready, 1)

            def copy_z(g, u, i, first):
                act.wait_ge(z_done, PIECES * (UNROLL * g + u) + i + 1)
                if not first:
                    act.wait_ge(z_stored[u], 16 * g)
                cols, bank_cols = piece(i)
                nc.scalar.copy(z_out[:, u, cols], z_ps[:, u % 2, i, bank_cols]).then_inc(z_copied[i], 1)

            def fill_b_tab(adapters):
                for n in range(adapters.start * HALVES, adapters.stop * HALVES, HALVES):
                    act.wait_ge(b_spread, n + 1)
                    nc.scalar.copy(b_tab[:, n // HALVES, 0:BANK], spread_bank(n)).then_inc(btab_ready[0], 1)

            for n in range(2):
                split_y(0, 0, n, True)
            for n in range(KT // KPB):
                act.wait_ge(at_turned, n + 1)
                nc.scalar.copy(atab[:, :, n * KPB:(n + 1) * KPB, 0:RANK].rearrange("p a k r -> p k a r"),
                               turn_bank(n).rearrange("p k (a r) -> p k a r", r=RANK)).then_inc(atab_hi, 1)
            for n in range(2, UNITS):
                split_y(0, 0, n, True)
            act.wait_ge(small_landed["b"], 16)
            nc.scalar.copy(b_flat[:, :, :, :], b_raw[:, :, :, :].rearrange("p a n r -> p n a r")).then_inc(b_flat_ready, 1)
            act.wait_ge(small_landed["ids"], 32)
            act.wait_ge(atab_ready, KT // KPB)
            stage_a(0, 0, True)
            split_x(0, 1, True)

            def step(g, u, first, last):
                g1, u1, first1 = g + (u + 1) // UNROLL, (u + 1) % UNROLL, first and u + 1 < UNROLL
                g2, u2 = g + (u + 2) // UNROLL, (u + 2) % UNROLL
                next1, next2 = not (last and u == UNROLL - 1), not (last and u >= UNROLL - 2)
                if next1:
                    split_y(g1, u1, 0, first1)
                split_r(g, u, first)
                if next1:
                    split_y(g1, u1, 1, first1)
                    stage_a(g1, u1, first1)
                if first and u == 0:
                    fill_b_tab(range(NA // 2))
                    fill_stack(g, u, first)
                    fill_b_tab(range(NA // 2, NA))
                    split_x(g2, u2, False)
                    split_y(g1, u1, 2, first1)
                    split_y(g1, u1, 3, first1)
                    copy_z(g, u, 0, first)
                else:
                    if next2:
                        split_x(g2, u2, False)
                    fill_stack(g, u, first)
                    if next1:
                        split_y(g1, u1, 2, first1)
                    copy_z(g, u, 0, first)
                    if next1:
                        split_y(g1, u1, 3, first1)
                copy_z(g, u, 2, first)

            for u in range(UNROLL):
                step(0, u, True, False)
            with act.Fori(1, GROUPS - 1) as g:
                for u in range(UNROLL):
                    step(g, u, False, False)
            for u in range(UNROLL):
                step(GROUPS - 1, u, False, True)

        @block.vector
        def _(dve):
            def bias_m(n):
                k, h = n // HALVES, n % HALVES
                if k // KPB == h:
                    dve.wait_ge(w_turned, n + 1)
                    tile = m_bank(n)[:, (k % KPB) * P:(k % KPB + 1) * P]
                    nc.vector.tensor_tensor(tile, tile, ident[:, :], ALU.add).then_inc(m_biased, 1)

            bias_m(0)
            for n in range(MBANKS):
                if n + 1 < MBANKS:
                    bias_m(n + 1)
                k, h = n // HALVES, n % HALVES
                cols = slice(h * BANK, (h + 1) * BANK)
                dve.wait_ge(m_hi_ready, n + 1)
                nc.vector.tensor_tensor(m_lo[:, k, cols], m_bank(n),
                                        m_hi[:, k, QUAD + h * BANK:QUAD + (h + 1) * BANK], ALU.subtract).then_inc(m_ready, 1)
                if n == MBANKS * 3 // 4 + 1:
                    dve.wait_ge(x_hi_ready, 1)
                    nc.vector.tensor_tensor(x_lo[:, 0, :], x_in[:, 0, :], x_hi[:, 0, :], ALU.subtract).then_inc(x_lo_ready, 1)

            def split_x(g, u):
                dve.wait_ge(x_hi_ready, UNROLL * g + u + 1)
                nc.vector.tensor_tensor(x_lo[:, u % 2, :], x_in[:, u, :], x_hi[:, u % 2, :], ALU.subtract)\
                  .then_inc(x_lo_ready, 1)

            def split_y(g, u, n):
                unit = UNITS * (UNROLL * g + u) + n
                tiles = slice(n * TPU, (n + 1) * TPU)
                hi, lo = y[:, u % 2, tiles, 0, :], y[:, u % 2, tiles, 1, :]
                dve.wait_ge(y_hi_ready, unit + 1)
                nc.vector.tensor_tensor(lo, y_ps[:, n % 2, :, 0, :], hi, ALU.subtract).then_inc(y_left, 1)
                dve.wait_ge(y_left, unit + 1)
                nc.vector.tensor_tensor(lo, y_ps[:, n % 2, :, 1, :], lo, ALU.add).then_inc(y_lo_ready, 1)

            def split_r(g, u):
                dve.wait_ge(r_hi_ready, UNROLL * g + u + 1)
                nc.vector.tensor_tensor(r_parts[:, NQ // 2:NQ, :],
                                        z_ps[:, u % 2, 0, 0:QUAD].unsqueeze(1).to_broadcast([P, NQ // 2, QUAD]),
                                        r_parts[:, 0:NQ // 2, :], ALU.subtract).then_inc(r_lo_ready, 1)

            def copy_z(g, u, i, first):
                dve.wait_ge(z_done, PIECES * (UNROLL * g + u) + i + 1)
                if not first:
                    dve.wait_ge(z_stored[u], 16 * g)
                cols, bank_cols = piece(i)
                nc.vector.tensor_copy(z_out[:, u, cols], z_ps[:, u % 2, i, bank_cols]).then_inc(z_copied[i], 1)

            def split_b():
                dve.wait_ge(small_landed["scale"], 16 * NA)
                for n in range(OT // KPB):
                    dve.wait_ge(bt_turned, n + 1)
                    bank = turn_bank(n)
                    hi, lo = [t[:, :].rearrange("p (c k) -> p k c", k=OT)[:, n * KPB:(n + 1) * KPB, :] for t in (bt_hi, bt_lo)]
                    nc.vector.tensor_scalar(bank, bank, scale[:, 0:1], None, ALU.mult).then_inc(bt_scaled, 1)
                    dve.wait_ge(bt_scaled, n + 1)
                    nc.vector.tensor_copy(hi, bank).then_inc(bt_split, 1)
                    dve.wait_ge(bt_split, 2 * n + 1)
                    nc.vector.tensor_tensor(lo, bank, hi, ALU.subtract).then_inc(bt_split, 1)

            def fill_b_tab():
                for n in range(1, NA * HALVES, HALVES):
                    dve.wait_ge(b_spread, n + 1)
                    nc.vector.tensor_copy(b_tab[:, n // HALVES, BANK:2 * BANK], spread_bank(n)).then_inc(btab_ready[1], 1)

            for n in range(2):
                split_y(0, 0, n)
            for n in range(KT // KPB):
                dve.wait_ge(atab_hi, n + 1)
                tiles = slice(n * KPB, (n + 1) * KPB)
                nc.vector.tensor_tensor(atab[:, :, tiles, RANK:QUAD].rearrange("p a k r -> p k a r"),
                                        turn_bank(n).rearrange("p k (a r) -> p k a r", r=RANK),
                                        atab[:, :, tiles, 0:RANK].rearrange("p a k r -> p k a r"), ALU.subtract)\
                  .then_inc(atab_ready, 1)
            for n in range(2, UNITS):
                split_y(0, 0, n)
            split_x(0, 1)
            split_b()

            def step(g, u, first, last):
                g1, u1 = g + (u + 1) // UNROLL, (u + 1) % UNROLL
                g2, u2 = g + (u + 2) // UNROLL, (u + 2) % UNROLL
                next1, next2 = not (last and u == UNROLL - 1), not (last and u >= UNROLL - 2)
                if next1:
                    split_y(g1, u1, 0)
                split_r(g, u)
                if next1:
                    split_y(g1, u1, 1)
                if first and u == 0:
                    fill_b_tab()
                if next2:
                    split_x(g2, u2)
                if next1:
                    split_y(g1, u1, 2)
                if first and u == 0:
                    split_y(g1, u1, 3)
                    copy_z(g, u, 1, first)
                else:
                    copy_z(g, u, 1, first)
                    if next1:
                        split_y(g1, u1, 3)

            for u in range(UNROLL):
                step(0, u, True, False)
            with dve.Fori(1, GROUPS - 1) as g:
                for u in range(UNROLL):
                    step(g, u, False, False)
            for u in range(UNROLL):
                step(GROUPS - 1, u, False, True)

        @block.tensor
        def _(pe):
            mm = nc.tensor.matmul

            pe.wait_ge(ident_ready, 2)
            for n in range(MBANKS):
                k, h = n // HALVES, n % HALVES
                if h == 0:
                    pe.wait_ge(w_landed[k], 16)
                if n >= RING:
                    pe.wait_ge(m_ready, n - RING + 1)
                for j in range(KPB):
                    turned = nc.tensor.transpose(m_bank(n)[:, j * P:(j + 1) * P], w_raw[:, k, h * KPB + j, :], ident[:, :])
                turned.then_inc(w_turned, 1)

            def first_layer(g, u, n, first):
                slot = u % 2
                if n == 0:
                    pe.wait_ge(w_staged, UNROLL * g + u + 1)
                    pe.wait_ge(x_lo_ready, UNROLL * g + u + 1)
                if not (first and u == 0 and n < 2):
                    pe.wait_ge(y_lo_ready, UNITS * (UNROLL * g + u) + n - 1)
                both = w_now[:, slot, :, :].rearrange("p h d -> p (h d)")
                for j in range(TPU):
                    k = n * TPU + j
                    cols = slice(k * P, (k + 1) * P)
                    yt = y_ps[:, n % 2, j, :, :].rearrange("p h c -> p (h c)")
                    mm(yt, x_hi[:, slot, cols], both, start=True, stop=False)
                    done = mm(yt, x_lo[:, slot, cols], both, start=False, stop=True)
                done.then_inc(y_done, 1)

            def second_layer(g, u, i, ks, first):
                slot = u % 2
                if i == 0:
                    pe.wait_ge(a_staged, UNROLL * g + u + 1)
                    pe.wait_ge(y_lo_ready, UNITS * (UNROLL * g + u) + ks[-1] // TPU + 1)
                if 0 in ks and not (first and u < 2):
                    pe.wait_ge(z_copied[i], UNROLL * g + u - 1)
                z, hi_cols = z_ps[:, slot, i, 0:PW], slice(PW * i, PW * (i + 1))
                lo_cols, bank_cols = piece(i)
                for k in ks:
                    mm(z, y[:, slot, k, 0, :], m_hi[:, k, hi_cols], start=(k == 0), stop=False)
                    mm(z_ps[:, slot, i, bank_cols], y[:, slot, k, 0, :], m_lo[:, k, lo_cols], start=False, stop=False,
                       skip_group_check=True)
                    done = mm(z, y[:, slot, k, 1, :], m_hi[:, k, hi_cols], start=False, stop=(k == KT - 1))
                if i == 0 and KT - 1 in ks:
                    done.then_inc(piece_done, 1)

            def turn_r(g, u, first):
                if first and u == 0:
                    pe.wait_ge(ident_r_ready, 1)
                pe.wait_ge(r_lo_ready, UNROLL * g + u + 1)
                mm(r_turn_bank(u % 2), r_parts[:, :, :].rearrange("p q r -> p (q r)"), ident_r[:, :],
                   start=False, stop=True, skip_group_check=True).then_inc(r_turned, 1)

            def add_rank_part(g, u, i):
                if i == 0:
                    pe.wait_ge(stack_ready, UNROLL * g + u + 1)
                    pe.wait_ge(b_staged, UNROLL * g + u + 1)
                cols, bank_cols = piece(i)
                mm(z_ps[:, u % 2, i, bank_cols], stack[:, :], b_now[:, u % 2, cols], start=False, stop=True,
                   skip_group_check=True).then_inc(z_done, 1)

            def turn_a():
                pe.wait_ge(small_landed["a"], 16)
                pe.wait_ge(m_ready, MBANKS)
                for k in range(KT):
                    turned = nc.tensor.transpose(turn_bank(k // KPB)[:, k % KPB, :], a_raw[:, k * P:(k + 1) * P], ident[:, :])
                    if k % KPB == KPB - 1:
                        turned.then_inc(at_turned, 1)

            def turn_b():
                pe.wait_ge(b_flat_ready, 1)
                pe.wait_ge(atab_ready, KT // KPB)
                for n in range(OT):
                    turned = nc.tensor.transpose(turn_bank(n // KPB)[:, n % KPB, :],
                                                 b_flat[:, n, :, :].rearrange("p a r -> p (a r)"), ident[:, :])
                    if n % KPB == KPB - 1:
                        turned.then_inc(bt_turned, 1)

            def spread_b(n):
                a, h = n // HALVES, n % HALVES
                cols = slice(h * BANK, (h + 1) * BANK)
                if n == 0:
                    pe.wait_ge(bt_split, 2 * HALVES)
                    pe.wait_ge(sel_ready, 2 * NQ)
                if a >= 1:
                    pe.wait_ge(btab_ready[h], a)
                mm(spread_bank(n), sel_hi[:, a, :, :, :].rearrange("p q h r -> p (q h r)"), bt_hi[:, cols],
                   start=True, stop=False)
                mm(spread_bank(n), sel_lo[:, a, :, :, :].rearrange("p q h r -> p (q h r)"), bt_lo[:, cols],
                   start=False, stop=True).then_inc(b_spread, 1)

            for n in range(2):
                first_layer(0, 0, n, True)
            turn_a()
            for n in range(2, UNITS):
                first_layer(0, 0, n, True)
            turn_b()

            front, back = range(KT // 2), range(KT // 2, KT)

            def first_step():
                second_layer(0, 0, 0, front, True)
                first_layer(0, 1, 0, True)
                second_layer(0, 0, 0, back, True)
                first_layer(0, 1, 1, True)
                for k in range(KT):
                    second_layer(0, 0, 1, [k], True)
                    for n in range(HALVES * k * NA // KT, HALVES * (k + 1) * NA // KT):
                        spread_b(n)
                    if k == KT // 2 - 1:
                        turn_r(0, 0, True)
                first_layer(0, 1, 2, True)
                second_layer(0, 0, 2, front, True)
                first_layer(0, 1, 3, True)
                second_layer(0, 0, 2, back, True)
                for i in range(PIECES):
                    add_rank_part(0, 0, i)

            def step(g, u, first, last):
                g1, u1, first1 = g + (u + 1) // UNROLL, (u + 1) % UNROLL, first and u + 1 < UNROLL
                next1 = not (last and u == UNROLL - 1)
                second_layer(g, u, 0, front, first)
                if next1:
                    first_layer(g1, u1, 0, first1)
                second_layer(g, u, 0, back, first)
                if next1:
                    first_layer(g1, u1, 1, first1)
                second_layer(g, u, 1, front, first)
                turn_r(g, u, first)
                second_layer(g, u, 1, back, first)
                if next1:
                    first_layer(g1, u1, 2, first1)
                add_rank_part(g, u, 0)
                add_rank_part(g, u, 1)
                second_layer(g, u, 2, front, first)
                if next1:
                    first_layer(g1, u1, 3, first1)
                second_layer(g, u, 2, back, first)
                add_rank_part(g, u, 2)

            first_step()
            for h in range(HALVES):
                pe.wait_ge(btab_ready[h], NA)
            for u in range(1, UNROLL):
                step(0, u, True, False)
            with pe.Fori(1, GROUPS - 1) as g:
                for u in range(UNROLL):
                    step(g, u, False, False)
            for u in range(UNROLL):
                step(GROUPS - 1, u, False, True)


INPUTS = ["x", "itok_B_0_7", "itok_B_0_6", "L0_cond_weights", "L1_cond_W", "L1_cond_A", "L1_cond_Bm",
          "L1_cond_scalings"]


def kernel(**inputs):
    import numpy as np
    import concourse.bacc as bacc
    from concourse.bass_utils import run_bass_kernel_spmd

    nc = bacc.Bacc("TRN2", target_bir_lowering=False, num_devices=1)
    arrays, args = {}, []
    for name in INPUTS:
        a = np.ascontiguousarray(inputs[name])
        arrays[f"in_{name}"] = a
        args.append(nc.dram_tensor(f"in_{name}", a.shape, mybir.dt.from_np(a.dtype), kind="ExternalInput").ap())
    shape = inputs["x"].shape
    args.append(nc.dram_tensor("out_0", shape, F32, kind="ExternalOutput").ap())
    cond_resid_kernel(nc, *args)
    r = run_bass_kernel_spmd(nc, [arrays], core_ids=[0])
    return r.results[0]["out_0"]
```
